# Optimizing a Trainium2 kernel written in Bass

```python
import numpy as np
import jax
import jax.numpy as jnp

def _softmax(x, axis=-1):
    return jax.nn.softmax(x, axis=axis)

def _gelu(x):
    return jax.nn.gelu(x, approximate=True)

def _silu(x):
    return jax.nn.silu(x)

def _sigmoid(x):
    return jax.nn.sigmoid(x)

def _layernorm(x, axis=-1, eps=1e-05):
    m = jnp.mean(x, axis=axis, keepdims=True)
    v = jnp.var(x, axis=axis, keepdims=True)
    return (x - m) / jnp.sqrt(v + eps)

def _scatter_add(tgt, idx, src, axis=0):
    return tgt.at[idx].add(src)

def _segment_sum(src, seg, n):
    return jax.ops.segment_sum(src, seg, n)
kernel_name = 'mk_xattn_ffn_d1_seqx_r4_d72389'

def setup_inputs(seed: int=0):
    np.random.seed(seed)
    _w = jnp.asarray

    def _rec_inputs():
        import jax
        import jax.numpy as jnp
        _rk = jax.random.key(seed)
        x = -0.0003929 + 0.9999 * jax.random.normal(jax.random.fold_in(_rk, 1), (16, 128, 1024), jnp.float32)
        _lenS = 128 - jax.random.randint(jax.random.fold_in(_rk, 7), (16,), 0, max(1, 128 // 4) + 1, jnp.int32)
        _lenS2 = 128 - jax.random.randint(jax.random.fold_in(_rk, 8), (16,), 0, max(1, 128 // 4) + 1, jnp.int32)
        _ctx_1024P = jax.random.normal(jax.random.fold_in(_rk, 11), (16, 16, 256), jnp.float32)
        _ctx_1024c = jax.random.dirichlet(jax.random.fold_in(_rk, 511), 0.3 * jnp.ones((16,), jnp.float32), (16, 128))
        _ctx_1024t = jnp.einsum('bsk,bkd->bsd', _ctx_1024c, _ctx_1024P)
        _ctx_1024t = _ctx_1024t * jax.lax.rsqrt(jnp.mean(jnp.square(_ctx_1024t)) + 1e-12) * 0.953939
        ctx_1024 = -1.39393e-06 + 0.999914 * (_ctx_1024t + 0.3 * jax.random.normal(jax.random.fold_in(_rk, 611), (16, 128, 256), jnp.float32))
        return (x, ctx_1024)
    x, ctx_1024 = _rec_inputs()

    def _L0_xattn_setup():
        import jax, jax.numpy as jnp
        import numpy as np
        import math
        DIM_V = 128
        key = jax.random.key(seed)
        k1, k2, k3, k4, k5, k6 = jax.random.split(key, 6)
        B, C, N, M = (8, DIM_V, 1024, 256)
        pcd_up = jax.random.normal(k1, (B, C, N), dtype=jnp.float32)
        pcd_down = jax.random.normal(k2, (B, C, M), dtype=jnp.float32)
        s = 1.0 / math.sqrt(C)
        Wq = jax.random.normal(k3, (C, C), dtype=jnp.float32) * s
        Wk = jax.random.normal(k4, (C, C), dtype=jnp.float32) * s
        Wv = jax.random.normal(k5, (C, C), dtype=jnp.float32) * s
        Wskip = jax.random.normal(k6, (C, C), dtype=jnp.float32) * s
        return {'pcd_up': pcd_up, 'pcd_down': pcd_down, 'Wq': Wq, 'Wk': Wk, 'Wv': Wv, 'Wskip': Wskip}
    _L0_xattn_all = _L0_xattn_setup()
    _L0_xattn_in = {k: v for k, v in _L0_xattn_all.items() if k in ('Wq', 'Wk', 'Wv', 'Wskip')}
    del _L0_xattn_all

    def _L0_ffn_setup():
        import jax, jax.numpy as jnp
        import numpy as np
        GROUP = 64

        def dequantize(W_q, scale, zero):
            out, half = W_q.shape
            hi = W_q >> 4 & 15
            lo = W_q & 15
            w = jnp.stack([hi, lo], axis=-1).reshape(out, half * 2).astype(scale.dtype)
            w = w.reshape(out, -1, GROUP)
            w = (w - zero[:, :, None]) * scale[:, :, None]
            return w.reshape(out, half * 2)
        key = jax.random.key(seed)
        ks = jax.random.split(key, 10)
        hidden, inter = (1024, 2752)
        B, S = (4, 256)
        x = jax.random.normal(ks[0], (B, S, hidden), dtype=jnp.float32)
        gate_Wq = jax.random.randint(ks[1], (inter, hidden // 2), 0, 64, dtype=jnp.int32)
        up_Wq = jax.random.randint(ks[2], (inter, hidden // 2), 0, 64, dtype=jnp.int32)
        down_Wq = jax.random.randint(ks[3], (hidden, inter // 2), 0, 64, dtype=jnp.int32)
        gate_scale = jax.random.uniform(ks[4], (inter, hidden // GROUP)) * 0.01 + 0.0001
        gate_zero = jax.random.uniform(ks[5], (inter, hidden // GROUP)) * 15.0
        up_scale = jax.random.uniform(ks[6], (inter, hidden // GROUP)) * 0.01 + 0.0001
        up_zero = jax.random.uniform(ks[7], (inter, hidden // GROUP)) * 15.0
        down_scale = jax.random.uniform(ks[8], (hidden, inter // GROUP)) * 0.01 + 0.0001
        down_zero = jax.random.uniform(ks[9], (hidden, inter // GROUP)) * 15.0
        return {'x': x, 'gate_Wq': gate_Wq, 'up_Wq': up_Wq, 'down_Wq': down_Wq, 'gate_scale': gate_scale, 'gate_zero': gate_zero, 'up_scale': up_scale, 'up_zero': up_zero, 'down_scale': down_scale, 'down_zero': down_zero}
    _L0_ffn_all = _L0_ffn_setup()
    _L0_ffn_in = {k: v for k, v in _L0_ffn_all.items() if k in ('gate_Wq', 'up_Wq', 'down_Wq', 'gate_scale', 'gate_zero', 'up_scale', 'up_zero', 'down_scale', 'down_zero')}
    del _L0_ffn_all
    return {'x': x, 'ctx_1024': ctx_1024, 'L0_xattn_Wq': _L0_xattn_in['Wq'], 'L0_xattn_Wk': _L0_xattn_in['Wk'], 'L0_xattn_Wv': _L0_xattn_in['Wv'], 'L0_xattn_Wskip': _L0_xattn_in['Wskip'], 'L0_ffn_gate_Wq': _L0_ffn_in['gate_Wq'], 'L0_ffn_up_Wq': _L0_ffn_in['up_Wq'], 'L0_ffn_down_Wq': _L0_ffn_in['down_Wq'], 'L0_ffn_gate_scale': _L0_ffn_in['gate_scale'], 'L0_ffn_gate_zero': _L0_ffn_in['gate_zero'], 'L0_ffn_up_scale': _L0_ffn_in['up_scale'], 'L0_ffn_up_zero': _L0_ffn_in['up_zero'], 'L0_ffn_down_scale': _L0_ffn_in['down_scale'], 'L0_ffn_down_zero': _L0_ffn_in['down_zero']}

def reference(x, ctx_1024, L0_xattn_Wq, L0_xattn_Wk, L0_xattn_Wv, L0_xattn_Wskip, L0_ffn_gate_Wq, L0_ffn_up_Wq, L0_ffn_down_Wq, L0_ffn_gate_scale, L0_ffn_gate_zero, L0_ffn_up_scale, L0_ffn_up_zero, L0_ffn_down_scale, L0_ffn_down_zero):
    import jax
    import jax.numpy as jnp

    def _L0_xattn_ref(pcd_up, pcd_down, Wq, Wk, Wv, Wskip):
        import jax, jax.numpy as jnp
        import numpy as np
        import math
        DIM_V = 128
        q = jnp.einsum('oc,bcn->bon', Wq, pcd_up)
        k = jnp.einsum('oc,bcm->bom', Wk, pcd_down)
        v = jnp.einsum('oc,bcm->bom', Wv, pcd_down)
        C = q.shape[1]
        scale = jnp.sqrt(jnp.asarray(C, dtype=q.dtype))
        energy = jnp.einsum('bcn,bcm->bnm', q, k) / scale
        attention = jax.nn.softmax(energy, axis=-1)
        x = jnp.einsum('bnm,bcm->bcn', attention, v)
        skip = jnp.einsum('oc,bcn->bon', Wskip, pcd_up)
        return skip + x

    def _L0_ffn_ref(x, gate_Wq, up_Wq, down_Wq, gate_scale, gate_zero, up_scale, up_zero, down_scale, down_zero):
        import jax, jax.numpy as jnp
        import numpy as np
        GROUP = 64

        def dequantize(W_q, scale, zero):
            out, half = W_q.shape
            hi = W_q >> 4 & 15
            lo = W_q & 15
            w = jnp.stack([hi, lo], axis=-1).reshape(out, half * 2).astype(scale.dtype)
            w = w.reshape(out, -1, GROUP)
            w = (w - zero[:, :, None]) * scale[:, :, None]
            return w.reshape(out, half * 2)
        Wg = dequantize(gate_Wq, gate_scale, gate_zero)
        Wu = dequantize(up_Wq, up_scale, up_zero)
        Wd = dequantize(down_Wq, down_scale, down_zero)
        g = jnp.einsum('bsh,ih->bsi', x, Wg)
        u = jnp.einsum('bsh,ih->bsi', x, Wu)
        h = jax.nn.silu(g) * u
        return jnp.einsum('bsi,hi->bsh', h, Wd)
    x = x + _L0_xattn_ref(_layernorm(x, axis=-1), ctx_1024, L0_xattn_Wq, L0_xattn_Wk, L0_xattn_Wv, L0_xattn_Wskip)
    x = x + _L0_ffn_ref(_layernorm(x, axis=-1), L0_ffn_gate_Wq, L0_ffn_up_Wq, L0_ffn_down_Wq, L0_ffn_gate_scale, L0_ffn_gate_zero, L0_ffn_up_scale, L0_ffn_up_zero, L0_ffn_down_scale, L0_ffn_down_zero)
    return x

_drawn_inputs = setup_inputs


def setup_inputs(seed=0):
    import zlib

    import numpy as np

    out = dict(_drawn_inputs(seed))
    spreads = {}
    factors = {}
    for name, (base, spread) in spreads.items():
        noise = np.random.default_rng([zlib.crc32(name.encode()), seed]).standard_normal(out[name].shape)
        drawn = base * np.exp(spread * noise) if base else spread * noise
        out[name] = jnp.asarray(drawn.astype(out[name].dtype))
    for name, factor in factors.items():
        out[name] = (out[name] * factor).astype(out[name].dtype)
    return out
```

```python
from contextlib import ExitStack

import numpy as np
import concourse.bass as bass
from concourse import mybir

F32 = mybir.dt.float32
F16 = mybir.dt.float16
BF16 = mybir.dt.bfloat16
I32 = mybir.dt.int32
ALU = mybir.AluOpType
ACT = mybir.ActivationFunctionType
X_AXIS = mybir.AxisListType.X

P = 128
B, C, N = 16, 128, 1024
M = 256
INTER = 2752
GROUP = 64
HALF_ROWS = P // 2
EPS = 1e-5
NT = N // P
NTH = NT // 2
H = N // 2
TOK = B * C
TB = TOK // 512
J = N // 256
PAIRS = -(-INTER // 256)
JOBS = 3 * PAIRS
JW = 1024
QG = P // (GROUP // 2)
NOUT = 512


def build(nc, x, ctx_in, wq, wk, wv_t, wskip_t, packed, grids, scales, zeros, out):
    ctx = ExitStack()
    with ctx:
        def sb(name, shape, dt):
            return ctx.enter_context(nc.sbuf_tensor(name, shape, dt))

        def sem(name):
            return ctx.enter_context(nc.semaphore(name))

        res = sb("res", [P, B, N], F32)
        xt = sb("xt", [P, 2, 2, J, TOK], F16)
        w_gu = sb("w_gu", [P, 2, 2, 2, 2, J, P], F16)
        raw = sb("raw", [P, JW], I32)
        grid = sb("grid", [P, 2, JW], F32)
        quant = sb("quant", [P, JW], I32)
        act_h = sb("act_h", [P, 2, 512], F32)
        pow2 = sb("pow2", [P, 16], F32)
        pow2_tmp = sb("pow2_tmp", [P, 8], F32)
        shared = sb("shared", [P, 6144], F32)
        h_hi = shared[:, 0:2048].bitcast(F16).rearrange("p (e t) -> p e t", e=2)
        h_lo = shared[:, 2048:4096].bitcast(BF16).rearrange("p (e t) -> p e t", e=2)
        w_d = shared[:, 4096:6144].bitcast(F16).rearrange("p (a e o) -> p a e o", a=2, e=2)
        xn = shared[:, 0:2048].rearrange("p (s n) -> p s n", s=2)
        prob = shared[:, 2048:4096].rearrange("p (t m) -> p t m", t=NT)
        prob_t = shared[:, 4096:6144].rearrange("p (f h n) -> p f h n", f=2, h=2)
        grids_all = shared[:, 0:6 * 344].rearrange("p (k n) -> p k n", k=6)
        xn2 = sb("xn2", [P, 2, N], F32)
        ctx_sb = sb("ctx_sb", [P, 2, M], F32)
        kk = sb("kk", [P, 2, M], F32)
        v_t = sb("v_t", [P, 2, 2, C], F32)
        w_att = sb("w_att", [P, 4, C], F32)
        qk_t = sb("qk_t", [P, C], F32)
        ident = sb("ident", [P, P], F32)
        stats = sb("stats", [P, 2, 2, 6], F32)
        mv = sb("mv", [P, 2, 2, 2], F32)
        var_eps = sb("var_eps", [P, 2], F32)
        rstd = sb("rstd", [P, 2, 2], F32)
        carrier = sb("carrier", [P, 1], F32)
        eps = sb("eps", [P, 1], F32)
        neg_half = sb("neg_half", [P, 1], F32)
        neg_max = sb("neg_max", [P, 2, NTH], F32)
        total = sb("total", [P, 2, NTH], F32)
        inv_total = sb("inv_total", [P, 2, NTH], F32)

        ps = ctx.enter_context(nc.psum_tensor("ps", [P, 8, 512], F32))
        ps_e = [ps[:, 2 * f:2 * f + 2, :].rearrange("p b (t m) -> p (b t) m", m=M) for f in range(2)]
        ps_t = ps[:, 4:6, :]
        ps_o = ps[:, 6, :]
        ps_m = ps[:, 7, :]

        s_weights_in = sem("s_weights_in")
        s_grids_in = sem("s_grids_in")
        s_x_in = [sem("s_x_in0"), sem("s_x_in1")]
        s_ctx_in = [sem("s_ctx_in0"), sem("s_ctx_in1")]
        s_job_in = sem("s_job_in")
        s_out = sem("s_out")
        s_const = sem("s_const")
        s_extreme = sem("s_extreme")
        s_extreme_all = sem("s_extreme_all")
        s_pow2 = sem("s_pow2")
        s_qk = sem("s_qk")
        s_qk_sb = sem("s_qk_sb")
        s_kv = sem("s_kv")
        s_kv_sb = sem("s_kv_sb")
        s_stat = [sem("s_stat1"), sem("s_stat2")]
        s_mv = [sem("s_mv1"), sem("s_mv2")]
        s_eps = sem("s_eps")
        s_rstd = [sem("s_rstd1"), sem("s_rstd2")]
        s_xn = sem("s_xn")
        s_xn2 = sem("s_xn2")
        s_energy = sem("s_energy")
        s_max = sem("s_max")
        s_exp = sem("s_exp")
        s_inv = sem("s_inv")
        s_prob = sem("s_prob")
        s_prob_t = sem("s_prob_t")
        s_prob_t_sb = sem("s_prob_t_sb")
        s_att = sem("s_att")
        s_res = sem("s_res")
        s_xt_ps = sem("s_xt_ps")
        s_xt_hi = sem("s_xt_hi")
        s_xt_lo = sem("s_xt_lo")
        s_nibble = sem("s_nibble")
        s_minus_zero = sem("s_minus_zero")
        s_weight = sem("s_weight")
        s_weight_hi = sem("s_weight_hi")
        s_weight_lo = sem("s_weight_lo")
        s_gate = sem("s_gate")
        s_up = sem("s_up")
        s_silu = sem("s_silu")
        s_h = sem("s_h")
        s_h_hi = sem("s_h_hi")
        s_h_lo = sem("s_h_lo")
        s_down = sem("s_down")
        s_acc = sem("s_acc")

        block = ctx.enter_context(nc.Block())

        def wait(eng, s, count):
            if not isinstance(count, int) or count > 0:
                eng.wait_ge(s, count)

        def attention_steps(eng, step):
            step(0, 0, True, False, False)
            step(0, 1, True, True, False)
            with eng.Fori(1, B // 2 - 1, 1) as k:
                step(k, 0, True, True, True)
                step(k, 1, True, True, True)
            step(B // 2 - 1, 0, True, True, True)
            step(B // 2 - 1, 1, True, True, True)
            step(B // 2, 0, False, True, True)
            step(B // 2, 1, False, False, True)

        @block.sync
        def _(sp):
            for k, w in enumerate((wq, wk, wv_t, wskip_t)):
                sp.dma_start(w_att[:, k, :], w[:, :]).then_inc(s_weights_in, 16)

            def load_batch(k, par, first):
                b = 2 * k + par
                if not first:
                    sp.wait_ge(s_x_in[par], 16 * k)
                    sp.wait_ge(s_kv, b - 1)
                sp.dma_start(ctx_sb[:, par, :], ctx_in[b, :, :]).then_inc(s_ctx_in[par], 16)
                sp.dma_start(res[:, b, :], x[b, :, :]).then_inc(s_x_in[par], 16)

            def load_job(n):
                wait(sp, s_weight_lo, 2 * n)
                sp.dma_start(raw[:, :], packed[n, :, :]).then_inc(s_job_in, 16)
                for g in range(QG):
                    rows = slice(g * P // QG, (g + 1) * P // QG)
                    sp.dma_start(grid[rows, :, :], grids[n, g:g + 1, :, :].to_broadcast([P // QG, 2, JW])
                                 ).then_inc(s_job_in, 16)

            load_batch(0, 0, True)
            load_batch(0, 1, True)
            for k in range(3):
                sp.dma_start(grids_all[:, k, :], scales[k, :, :]).then_inc(s_grids_in, 16)
                sp.dma_start(grids_all[:, 3 + k, :], zeros[k, :, :]).then_inc(s_grids_in, 16)
            load_job(0)
            with sp.Fori(1, B // 2, 1) as k:
                load_batch(k, 0, False)
                load_batch(k, 1, False)
            with sp.Fori(1, JOBS, 1) as n:
                load_job(n)
            for t in range(B):
                sp.wait_ge(s_acc, 2 * B * (PAIRS - 1) + 2 * t + 2)
                sp.dma_start(out[t, :, :], res[:, t, :]).then_inc(s_out, 16)
            sp.wait_ge(s_out, 16 * B)

        @block.gpsimd
        def _(pool):
            pool.memset(neg_half[:, :], -0.5).then_inc(s_const, 1)
            pool.memset(ident[:, :], 0.0).then_inc(s_const, 1)
            pool.memset(eps[:, :], EPS).then_inc(s_const, 1)
            pool.wait_ge(s_const, 3)
            pool.affine_select(out=ident[:, :], in_=ident[:, :], compare_op=ALU.not_equal, fill=1.0,
                               base=0, pattern=[[-1, P]], channel_multiplier=1).then_inc(s_const, 1)
            pool.wait_ge(s_extreme, 1)
            pool.partition_all_reduce(pow2_tmp[:, 0:6], pow2[:, 0:6], P,
                                      bass.bass_isa.ReduceOp.max).then_inc(s_extreme_all, 1)

            def inverse_deviation(which, b, par, nth):
                pool.wait_ge(s_mv[which], b + 1)
                pool.tensor_tensor(var_eps[:, which:which + 1], mv[:, which, par, 1:2], eps[:, :],
                                   ALU.add).then_inc(s_eps, 1)
                pool.wait_ge(s_eps, nth)
                pool.tensor_tensor(rstd[:, which, par:par + 1], var_eps[:, which:which + 1],
                                   neg_half[:, :], ALU.pow).then_inc(s_rstd[which], 1)

            inverse_deviation(0, 0, 0, 1)
            inverse_deviation(0, 1, 1, 2)
            with pool.Fori(1, B // 2, 1) as k:
                for par in (0, 1):
                    b = 2 * k + par
                    inverse_deviation(0, b, par, 2 * b - 1)
                    inverse_deviation(1, b - 2, par, 2 * b)
            inverse_deviation(1, B - 2, 0, 2 * B - 1)
            inverse_deviation(1, B - 1, 1, 2 * B)

        @block.tensor
        def _(pe):
            def keys_values(k, par):
                b = 2 * k + par
                pe.wait_ge(s_ctx_in[par], 16 * k + 16)
                wait(pe, s_xt_lo, 2 * b - 4)
                pe.matmul(ps_m[:, 0:M], qk_t[:, :], ctx_sb[:, par, :], start=True, stop=True)
                for h in range(2):
                    mm = pe.matmul(ps_m[:, M + C * h:M + C * h + C], ctx_sb[:, par, P * h:P * h + P],
                                   w_att[:, 2, :], start=True, stop=True)
                mm.then_inc(s_kv, 1)

            def probs_transposed(b, f):
                pe.wait_ge(s_prob, 2 * b + f + 1)
                wait(pe, s_prob_t_sb, 2 * b + f)
                for h in range(2):
                    for t in range(NTH):
                        mm = pe.transpose(ps_t[:, h, P * t:P * t + P],
                                          prob[:, NTH * f + t, P * h:P * h + P], ident[:, :])
                mm.then_inc(s_prob_t, 1)

            def energies(b, par, f):
                if f == 0:
                    pe.wait_ge(s_xn, b + 1)
                    pe.wait_ge(s_kv_sb, b + 1)
                wait(pe, s_exp, 2 * b - 1 + f)
                for t in range(NTH):
                    n = H * f + P * t
                    mm = pe.matmul(ps_e[f][:, t, :], xn[:, par, n:n + P], kk[:, par, :],
                                   start=True, stop=True)
                mm.then_inc(s_energy, 1)

            def rows_transposed(b, par, f):
                if f == 0:
                    pe.wait_ge(s_xn2, b + 1)
                    wait(pe, s_kv_sb, min(b + 3, B) if isinstance(b, int) else b + 3)
                else:
                    pe.wait_ge(s_xt_lo, 2 * b + 1)
                for j in range(J):
                    mm = pe.transpose(ps_m[:, P * j:P * j + P],
                                      xn2[:, par, 256 * j + f:256 * j + 256:2], ident[:, :])
                mm.then_inc(s_xt_ps, 1)

            def values(b, par, f):
                wait(pe, s_res, 2 * b + f)
                pe.matmul(ps_o, w_att[:, 3, :], xn[:, par, H * f:H * f + H], start=True, stop=False)
                pe.wait_ge(s_prob_t_sb, 2 * b + f + 1)
                pe.matmul(ps_o, v_t[:, par, 0, :], prob_t[:, f, 0, :], start=False, stop=False)
                pe.matmul(ps_o, v_t[:, par, 1, :], prob_t[:, f, 1, :], start=False, stop=True
                          ).then_inc(s_att, 1)

            pe.wait_ge(s_weights_in, 64)
            pe.matmul(ps_m[:, 0:C], w_att[:, 1, :], w_att[:, 0, :], start=True, stop=True).then_inc(s_qk, 1)
            pe.wait_ge(s_qk_sb, 1)
            pe.wait_ge(s_const, 4)
            keys_values(0, 0)

            def step(k, par, a, b, c):
                i = 2 * k + par
                for f in range(2):
                    if b:
                        probs_transposed(i - 1, f)
                    if a:
                        energies(i, par, f)
                    if c:
                        rows_transposed(i - 2, par, f)
                    if b:
                        values(i - 1, 1 - par, f)
                if a and not (isinstance(i, int) and i == B - 1):
                    keys_values(k + par, 1 - par)

            attention_steps(pe, step)

            def gate_up(pair, e, tb):
                u = 2 * TB * pair + TB * e + tb
                cols = slice(512 * tb, 512 * tb + 512)
                if tb == 0:
                    pe.wait_ge(s_weight_lo, 2 * (3 * pair + e) + 2)
                for k, (ready, free) in enumerate(((s_gate, s_silu), (s_up, s_h))):
                    bank = ps[:, 2 * (tb % 2) + k, :]
                    wait(pe, free, u - 1)
                    n = 0
                    for odd in range(2):
                        for j in range(J):
                            for wp, xp in ((0, 0), (0, 1), (1, 0)):
                                mm = pe.matmul(bank, w_gu[:, e, wp, odd, k, j, :], xt[:, xp, odd, j, cols],
                                               start=(n == 0), stop=(n == 6 * J - 1))
                                n += 1
                    mm.then_inc(ready, 1)

            def down(pair, t):
                for oh in range(2):
                    g = 2 * B * pair + 2 * t + oh
                    bank = ps[:, 4 + (2 * t + oh) % 4, :]
                    wait(pe, s_acc, g - 3)
                    n = 0
                    for e in range(2):
                        rows = slice(P * t, P * t + P)
                        o = slice(NOUT * oh, NOUT * oh + NOUT)
                        for h, wp in ((h_hi, 0), (h_hi, 1), (h_lo, 0)):
                            mm = pe.matmul(bank, h[:, e, rows], w_d[:, wp, e, o], start=(n == 0), stop=(n == 5))
                            n += 1
                    mm.then_inc(s_down, 1)

            def ffn_pair(pair):
                for e in range(2):
                    for tb in range(TB):
                        gate_up(pair, e, tb)
                pe.wait_ge(s_weight_lo, 6 * pair + 6)
                for t in range(B):
                    if t % 4 == 0:
                        pe.wait_ge(s_h_lo, 2 * TB * pair + TB + t // 4 + 1)
                    down(pair, t)

            pe.wait_ge(s_xt_lo, 2 * B)
            ffn_pair(0)
            with pe.Fori(1, PAIRS, 1) as pair:
                ffn_pair(pair)

        @block.scalar
        def _(act):
            act.wait_ge(s_qk, 1)
            act.copy(qk_t[:, :], ps_m[:, 0:C]).then_inc(s_qk_sb, 1)

            def keys_values_out(b, par):
                act.wait_ge(s_kv, b + 1)
                act.mul(kk[:, par, :], ps_m[:, 0:M], float(C) ** -0.5)
                act.copy(v_t[:, par, :, :], ps_m[:, M:M + 2 * C].rearrange("p (h c) -> p h c", h=2)
                         ).then_inc(s_kv_sb, 1)

            def step(k, par, a, b, c):
                i = 2 * k + par
                for f in range(2):
                    if b:
                        act.wait_ge(s_prob_t, 2 * (i - 1) + f + 1)
                        act.copy(prob_t[:, f, :, :], ps_t).then_inc(s_prob_t_sb, 1)
                    if a:
                        act.wait_ge(s_max, 2 * i + f + 1)
                        for t in range(NTH):
                            ex = act.activation(prob[:, NTH * f + t, :], ps_e[f][:, t, :], ACT.Exp,
                                                bias=neg_max[:, f, t:t + 1], accum_out=total[:, f, t:t + 1])
                        ex.then_inc(s_exp, 1)
                    if c:
                        r = (i - 2) * C
                        act.wait_ge(s_xt_ps, 2 * (i - 2) + f + 1)
                        act.copy(xt[:, 0, f, :, bass.ds(r, C)],
                                 ps_m.rearrange("p (j r) -> p j r", j=J)).then_inc(s_xt_hi, 1)
                if a and not (isinstance(i, int) and i == B - 1):
                    keys_values_out(i + 1, 1 - par)

            def weight_hi(n, kind, nib):
                act.wait_ge(s_weight, 2 * n + nib + 1)
                src = (quant, raw)[nib][:, :].bitcast(F32)
                dst = w_d[:, 0, nib, :] if kind == 2 else w_gu[:, kind, 0, nib, :, :, :].rearrange("p k j m -> p (k j m)")
                act.copy(dst, src).then_inc(s_weight_hi, 1)

            keys_values_out(0, 0)
            for nib in range(2):
                weight_hi(0, 0, nib)
            attention_steps(act, step)
            for nib in range(2):
                weight_hi(1, 1, nib)

            def unit(pair, e, tb):
                u = 2 * TB * pair + TB * e + tb
                act.wait_ge(s_gate, u + 1)
                wait(act, s_h_lo, u - 1)
                act.activation(act_h[:, tb % 2, :], ps[:, 2 * (tb % 2), :], ACT.Silu,
                               scale=pow2[:, 8:9]).then_inc(s_silu, 1)
                act.wait_ge(s_h, u + 1)
                act.copy(h_hi[:, e, 512 * tb:512 * tb + 512], act_h[:, tb % 2, :]).then_inc(s_h_hi, 1)

            def ffn_pair(pair, last):
                for e in range(2):
                    for tb in range(TB):
                        unit(pair, e, tb)
                        if tb in (0, 1) and e == 0:
                            wait(act, s_down, 2 * B * pair)
                            weight_hi(3 * pair + 2, 2, tb)
                        if tb in (0, 1) and e == 1 and not last:
                            act.wait_ge(s_up, 2 * TB * pair + TB)
                            weight_hi(3 * pair + 3, 0, tb)
                if not last:
                    act.wait_ge(s_up, 2 * TB * pair + 2 * TB)
                    for nib in range(2):
                        weight_hi(3 * pair + 4, 1, nib)

            ffn_pair(0, False)
            with act.Fori(1, PAIRS - 1, 1) as pair:
                ffn_pair(pair, False)
            ffn_pair(PAIRS - 1, True)

        @block.vector
        def _(dve):
            dve.wait_ge(s_grids_in, 96)
            for k in range(6):
                dve.tensor_reduce(pow2[:, k:k + 1], grids_all[:, k, :], X_AXIS, ALU.max,
                                  apply_absolute_value=True)
            dve.tensor_reduce(pow2[:, 11:12], grids_all[:, 0, 0:1], X_AXIS, ALU.max).then_inc(s_extreme, 1)

            def after(ins):
                count[0] += 1
                ins.then_inc(s_pow2, 1)
                dve.wait_ge(s_pow2, count[0])

            count = [0]
            dve.wait_ge(s_extreme_all, 1)
            after(dve.tensor_tensor(pow2_tmp[:, 0:4:3], pow2_tmp[:, 0:4:3], pow2_tmp[:, 1:5:3], ALU.max))
            after(dve.tensor_scalar(pow2_tmp[:, 3:6:2], pow2_tmp[:, 3:6:2], 15.0, None, ALU.add))
            after(dve.tensor_tensor(pow2_tmp[:, 0:3:2], pow2_tmp[:, 0:3:2], pow2_tmp[:, 3:6:2], ALU.mult))
            after(dve.tensor_scalar(pow2_tmp[:, 6:8], pow2_tmp[:, 0:3:2], 2.0 ** -60, None, ALU.max))
            bits = pow2_tmp[:, 6:8].bitcast(I32)
            after(dve.tensor_scalar(bits, bits, 0x7F800000, None, ALU.bitwise_and))
            after(dve.reciprocal(pow2[:, 6:8], pow2_tmp[:, 6:8]))
            after(dve.tensor_scalar(pow2[:, 9:10], pow2[:, 6:7], 2.0 ** -21, None, ALU.mult))
            after(dve.tensor_scalar(pow2[:, 6:8], pow2[:, 6:8], 2.0 ** 14, None, ALU.mult))
            after(dve.tensor_scalar(pow2[:, 8:9], pow2_tmp[:, 6:7], 2.0 ** -14, None, ALU.mult))
            after(dve.tensor_tensor(pow2[:, 10:11], pow2_tmp[:, 6:7], pow2_tmp[:, 6:7], ALU.mult))
            after(dve.tensor_scalar(pow2[:, 10:11], pow2[:, 10:11], pow2_tmp[:, 7:8], 2.0 ** -7,
                                    ALU.mult, ALU.mult))

            def wait_carrier():
                dve.memset(carrier[:, :], 0.0)

            def row_stats(which, b, par, src):
                wait_carrier()
                for k in range(2):
                    st = dve.bn_stats(stats[:, which, k, :], src[:, 512 * k:512 * k + 512])
                st.then_inc(s_stat[which], 1)
                dve.wait_ge(s_stat[which], b + 1)
                wait_carrier()
                dve.bn_aggr(mv[:, which, par, :], stats[:, which, :, :].rearrange("p a b -> p (a b)")
                            ).then_inc(s_mv[which], 1)

            def normalize(which, b, par, dst, src, done):
                dve.wait_ge(s_rstd[which], b + 1)
                dve.tensor_scalar(dst, src, mv[:, which, par, 0:1], rstd[:, which, par:par + 1],
                                  ALU.subtract, ALU.mult).then_inc(done, 1)

            def row(b):
                return res[:, b, :]

            def x_arrived(k, par):
                dve.wait_ge(s_x_in[par], 16 * k + 16)

            def maxima(b, f):
                dve.wait_ge(s_energy, 2 * b + f + 1)
                dve.tensor_reduce(neg_max[:, f, :], ps_e[f], X_AXIS, ALU.max, negate=True).then_inc(s_max, 1)

            def normalize_probs(b, f):
                dve.wait_ge(s_exp, 2 * b + f + 1)
                dve.reciprocal(inv_total[:, f, :], total[:, f, :]).then_inc(s_inv, 1)
                dve.wait_ge(s_inv, 2 * b + f + 1)
                for t in range(NTH):
                    pr = prob[:, NTH * f + t, :]
                    pn = dve.tensor_scalar(pr, pr, inv_total[:, f, t:t + 1], None, ALU.mult)
                pn.then_inc(s_prob, 1)

            def rows_lo(b, f):
                dve.wait_ge(s_xt_hi, 2 * b + f + 1)
                r = b * C
                dve.tensor_tensor(xt[:, 1, f, :, bass.ds(r, C)], ps_m.rearrange("p (j r) -> p j r", j=J),
                                  xt[:, 0, f, :, bass.ds(r, C)], ALU.subtract).then_inc(s_xt_lo, 1)

            def add_attention(b, f):
                part = res[:, b, H * f:H * f + H]
                dve.tensor_tensor(part, ps_o, part, ALU.add).then_inc(s_res, 1)

            def step(k, par, a, b, c):
                i = 2 * k + par
                nxt = a and not (isinstance(i, int) and i == B - 1)
                if c:
                    normalize(1, i - 2, par, xn2[:, par, :], row(i - 2), s_xn2)
                if a:
                    maxima(i, 0)
                if nxt and not (isinstance(i, int) and i == 0):
                    x_arrived(k + par, 1 - par)
                    row_stats(0, i + 1, 1 - par, row(i + 1))
                if c:
                    rows_lo(i - 2, 0)
                if b:
                    dve.wait_ge(s_att, 2 * (i - 1) + 1)
                    add_attention(i - 1, 0)
                if a:
                    normalize_probs(i, 0)
                    maxima(i, 1)
                if c:
                    rows_lo(i - 2, 1)
                if b:
                    dve.wait_ge(s_att, 2 * (i - 1) + 2)
                if nxt:
                    normalize(0, i + 1, 1 - par, xn[:, 1 - par, :], row(i + 1), s_xn)
                if b:
                    add_attention(i - 1, 1)
                    dve.wait_ge(s_res, 2 * (i - 1) + 2)
                    row_stats(1, i - 1, 1 - par, row(i - 1))
                if a:
                    normalize_probs(i, 1)

            def weights(n, kind, nib, part):
                t_int = (quant, raw)[nib][:, :]
                t = t_int.bitcast(F32)
                k = 2 * n + nib + 1
                if part == 0:
                    dve.wait_ge(s_job_in, 16 * (1 + QG) * (n + 1))
                    if nib == 0:
                        dve.tensor_scalar(t_int, raw[:, :], 4, 15, ALU.logical_shift_right,
                                          ALU.bitwise_and).then_inc(s_nibble, 1)
                    else:
                        dve.tensor_scalar(t_int, raw[:, :], 15, None, ALU.bitwise_and).then_inc(s_nibble, 1)
                if part == 1:
                    dve.wait_ge(s_nibble, k)
                    dve.tensor_tensor(t, t_int, grid[:, 1, :], ALU.subtract).then_inc(s_minus_zero, 1)
                if part == 2:
                    a = 7 if kind == 2 else 6
                    dve.wait_ge(s_minus_zero, k)
                    dve.scalar_tensor_tensor(out=t, in0=t, scalar=pow2[:, a:a + 1], in1=grid[:, 0, :],
                                             op0=ALU.mult, op1=ALU.mult).then_inc(s_weight, 1)
                if part == 3:
                    dve.wait_ge(s_weight_hi, k)
                    if kind == 2:
                        hi, lo = (w_d[:, wp, nib, :] for wp in range(2))
                    else:
                        hi, lo = (w_gu[:, kind, wp, nib, :, :, :].rearrange("p k j m -> p (k j m)")
                                  for wp in range(2))
                    dve.tensor_tensor(lo, t, hi, ALU.subtract).then_inc(s_weight_lo, 1)

            x_arrived(0, 0)
            row_stats(0, 0, 0, row(0))
            normalize(0, 0, 0, xn[:, 0, :], row(0), s_xn)
            x_arrived(0, 1)
            row_stats(0, 1, 1, row(1))
            for nib in range(2):
                for part in range(4):
                    weights(0, 0, nib, part)
            attention_steps(dve, step)
            for nib in range(2):
                for part in range(4):
                    weights(1, 1, nib, part)

            def unit(pair, e, tb):
                u = 2 * TB * pair + TB * e + tb
                a = act_h[:, tb % 2, :]
                cols = slice(512 * tb, 512 * tb + 512)
                dve.wait_ge(s_silu, u + 1)
                dve.wait_ge(s_up, u + 1)
                dve.scalar_tensor_tensor(out=a, in0=ps[:, 2 * (tb % 2) + 1, :], scalar=pow2[:, 9:10], in1=a,
                                         op0=ALU.mult, op1=ALU.mult).then_inc(s_h, 1)
                dve.wait_ge(s_h_hi, u + 1)
                dve.tensor_tensor(h_lo[:, e, cols], a, h_hi[:, e, cols], ALU.subtract).then_inc(s_h_lo, 1)

            def add_down(pair, k):
                t, oh = k // 2, k % 2
                part = res[:, t, NOUT * oh:NOUT * oh + NOUT]
                dve.wait_ge(s_down, 2 * B * pair + k + 1)
                dve.scalar_tensor_tensor(out=part, in0=ps[:, 4 + k % 4, :], scalar=pow2[:, 10:11], in1=part,
                                         op0=ALU.mult, op1=ALU.add).then_inc(s_acc, 1)

            def ffn_pair(pair, last):
                for e in range(2):
                    for tb in range(TB):
                        unit(pair, e, tb)
                        if tb in (0, 1) and e == 0:
                            for part in range(4):
                                weights(3 * pair + 2, 2, tb, part)
                        if tb in (0, 1) and e == 1 and not last:
                            for part in range(4):
                                weights(3 * pair + 3, 0, tb, part)
                for k in range(2 * B):
                    add_down(pair, k)
                    if k % 4 == 3 and not last:
                        weights(3 * pair + 4, 1, k // 16, k // 4 % 4)

            ffn_pair(0, False)
            with dve.Fori(1, PAIRS - 1, 1) as pair:
                ffn_pair(pair, False)
            ffn_pair(PAIRS - 1, True)


def kernel(x, ctx_1024, L0_xattn_Wq, L0_xattn_Wk, L0_xattn_Wv, L0_xattn_Wskip, L0_ffn_gate_Wq, L0_ffn_up_Wq,
           L0_ffn_down_Wq, L0_ffn_gate_scale, L0_ffn_gate_zero, L0_ffn_up_scale, L0_ffn_up_zero,
           L0_ffn_down_scale, L0_ffn_down_zero):
    import concourse.bacc as bacc
    from concourse.bass_utils import run_bass_kernel_spmd

    pad = PAIRS * 256

    def gate_up_layout(gate, up, rows, groups):
        a = np.stack([np.asarray(gate), np.asarray(up)])
        full = np.zeros((2, pad, a.shape[2]), a.dtype)
        full[:, :INTER] = a
        a = full.reshape(2, PAIRS, P, 2, groups, rows)
        return a.transpose(1, 3, 5, 0, 4, 2).reshape(PAIRS, 2, rows, JW)

    def down_layout(a, rows):
        a = np.asarray(a)
        full = np.zeros((PAIRS * rows, N), a.dtype)
        full[:a.shape[1]] = a.T
        return full.reshape(PAIRS, 1, rows, N)

    packed = np.concatenate([gate_up_layout(L0_ffn_gate_Wq, L0_ffn_up_Wq, P, J),
                             down_layout(L0_ffn_down_Wq, P)], axis=1).reshape(JOBS, P, JW)
    grids = np.stack([np.concatenate([gate_up_layout(g, u, QG, J), down_layout(d, QG)], axis=1)
                      for g, u, d in ((L0_ffn_gate_scale, L0_ffn_up_scale, L0_ffn_down_scale),
                                      (L0_ffn_gate_zero, L0_ffn_up_zero, L0_ffn_down_zero))], axis=3)
    arrays = {
        "x": np.asarray(x),
        "ctx": np.asarray(ctx_1024),
        "wq": np.asarray(L0_xattn_Wq),
        "wk": np.asarray(L0_xattn_Wk),
        "wv_t": np.asarray(L0_xattn_Wv).T,
        "wskip_t": np.asarray(L0_xattn_Wskip).T,
        "packed": packed,
        "grids": grids.reshape(JOBS, QG, 2, JW),
        "scales": np.stack([np.asarray(a).reshape(P, -1) for a in
                            (L0_ffn_gate_scale, L0_ffn_up_scale, L0_ffn_down_scale)]),
        "zeros": np.stack([np.asarray(a).reshape(P, -1) for a in
                           (L0_ffn_gate_zero, L0_ffn_up_zero, L0_ffn_down_zero)]),
    }
    arrays = {k: np.ascontiguousarray(a) for k, a in arrays.items()}
    nc = bacc.Bacc("TRN2", target_bir_lowering=False, num_devices=1)
    args = [nc.dram_tensor(k, a.shape, mybir.dt.from_np(a.dtype), kind="ExternalInput").ap()
            for k, a in arrays.items()]
    out = nc.dram_tensor("out", (B, C, N), F32, kind="ExternalOutput").ap()
    build(nc, *args, out)
    r = run_bass_kernel_spmd(nc, [arrays], core_ids=[0])
    return r.results[0]["out"]
```

```python
from contextlib import ExitStack

import numpy as np
import concourse.bass as bass
from concourse import mybir

F32 = mybir.dt.float32
F16 = mybir.dt.float16
BF16 = mybir.dt.bfloat16
I32 = mybir.dt.int32
ALU = mybir.AluOpType
ACT = mybir.ActivationFunctionType
X_AXIS = mybir.AxisListType.X

P = 128
B, C, N = 16, 128, 1024
M = 256
INTER = 2752
GROUP = 64
EPS = 1e-5
NT = N // P
NTH = NT // 2
H = N // 2
TOK = B * C
TB = TOK // 512
J = N // 256
PAIRS = INTER // 256
JOBS = 3 * PAIRS + 4
HALF = P // 2
WARM_UP = 10
EARLY = 1
JW = 1024
QG = P // (GROUP // 2)
NOUT = 512


def build(nc, x, ctx_in, att_weights, packed, grids, scales, zeros, out):
    ctx = ExitStack()
    with ctx:
        def sb(name, shape, dt):
            return ctx.enter_context(nc.sbuf_tensor(name, shape, dt))

        def sem(name):
            return ctx.enter_context(nc.semaphore(name))

        res = sb("res", [P, B, N], F32)
        xt = sb("xt", [P, 2, 2, J, TOK], F16)
        w_gu = sb("w_gu", [P, 2, 2, 2, 2, J, P], F16)
        grids_all = w_gu[:, :, :, :, :, :, :].rearrange("p s a e k j m -> p (s a e k j m)")[:, 0:12 * 344].bitcast(
            F32).rearrange("p (k n) -> p k n", k=6)
        raw = sb("raw", [P, JW], I32)
        grid = sb("grid", [P, 2, JW], F32)
        quant = sb("quant", [P, JW], I32)
        act_h = sb("act_h", [P, 2, 512], F32)
        pow2 = sb("pow2", [P, 16], F32)
        pow2_tmp = sb("pow2_tmp", [P, 8], F32)
        shared = sb("shared", [P, 6144], F32)
        h_hi = shared[:, 0:2048].bitcast(F16).rearrange("p (e t) -> p e t", e=2)
        h_lo = shared[:, 2048:4096].bitcast(BF16).rearrange("p (e t) -> p e t", e=2)
        w_d = shared[:, 4096:6144].bitcast(F16).rearrange("p (a e o) -> p a e o", a=2, e=2)
        xn = shared[:, 0:2048].rearrange("p (s n) -> p s n", s=2)
        prob = shared[:, 2048:4096].rearrange("p (t m) -> p t m", t=NT)
        prob_t = shared[:, 4096:6144].rearrange("p (f h n) -> p f h n", f=2, h=2)
        xn2 = sb("xn2", [P, 2, N], F32)
        ctx_sb = sb("ctx_sb", [P, 2, M], F32)
        kk = sb("kk", [P, 2, M], F32)
        v_t = sb("v_t", [P, 2, 2, C], F32)
        w_att = sb("w_att", [P, 4, C], F32)
        qk_t = sb("qk_t", [P, C], F32)
        ident = sb("ident", [P, P], F32)
        stats = sb("stats", [P, 2, 2, 6], F32)
        mv = sb("mv", [P, 2, 2, 2], F32)
        var_eps = sb("var_eps", [P, 2], F32)
        rstd = sb("rstd", [P, 2, 2], F32)
        carrier = sb("carrier", [P, 1], F32)
        eps = sb("eps", [P, 1], F32)
        neg_half = sb("neg_half", [P, 1], F32)
        neg_max = sb("neg_max", [P, 2, NTH], F32)
        total = sb("total", [P, 2, NTH], F32)
        inv_total = sb("inv_total", [P, 2, NTH], F32)

        ps = ctx.enter_context(nc.psum_tensor("ps", [P, 8, 512], F32))
        ps_e = [ps[:, 2 * f:2 * f + 2, :].rearrange("p b (t m) -> p (b t) m", m=M) for f in range(2)]
        ps_t = ps[:, 4:6, :]
        ps_o = ps[:, 6, :]
        ps_m = ps[:, 7, :]

        s_weights_in = sem("s_weights_in")
        s_grids_in = sem("s_grids_in")
        s_x_in = [sem("s_x_in0"), sem("s_x_in1")]
        s_ctx_in = [sem("s_ctx_in0"), sem("s_ctx_in1")]
        s_job_in = sem("s_job_in")
        s_out = sem("s_out")
        s_const = sem("s_const")
        s_extreme = sem("s_extreme")
        s_extreme_all = sem("s_extreme_all")
        s_pow2 = sem("s_pow2")
        s_qk = sem("s_qk")
        s_qk_sb = sem("s_qk_sb")
        s_kv = sem("s_kv")
        s_kk_sb = sem("s_kk_sb")
        s_vt_sb = sem("s_vt_sb")
        s_stat = [sem("s_stat1"), sem("s_stat2")]
        s_mv = [sem("s_mv1"), sem("s_mv2")]
        s_eps = sem("s_eps")
        s_rstd = [sem("s_rstd1"), sem("s_rstd2")]
        s_xn = sem("s_xn")
        s_xn2 = sem("s_xn2")
        s_energy = sem("s_energy")
        s_max = sem("s_max")
        s_exp = sem("s_exp")
        s_inv = sem("s_inv")
        s_prob = sem("s_prob")
        s_prob_t = sem("s_prob_t")
        s_prob_t_sb = sem("s_prob_t_sb")
        s_att = sem("s_att")
        s_res = sem("s_res")
        s_xt_ps = sem("s_xt_ps")
        s_xt_hi = sem("s_xt_hi")
        s_xt_lo = sem("s_xt_lo")
        s_nibble = sem("s_nibble")
        s_minus_zero = sem("s_minus_zero")
        s_weight = sem("s_weight")
        s_weight_hi = sem("s_weight_hi")
        s_weight_lo = sem("s_weight_lo")
        s_gate = sem("s_gate")
        s_up = sem("s_up")
        s_silu = sem("s_silu")
        s_h = sem("s_h")
        s_h_hi = sem("s_h_hi")
        s_h_lo = sem("s_h_lo")
        s_down = sem("s_down")
        s_acc = sem("s_acc")

        block = ctx.enter_context(nc.Block())

        def wait(eng, s, count):
            if not isinstance(count, int) or count > 0:
                eng.wait_ge(s, count)

        def stages(i):
            if isinstance(i, int):
                return i < B, 1 <= i <= B, 2 <= i < B + 2, 3 <= i < B + 3, i + 1 < B
            return True, True, True, True, True

        @block.sync
        def _(sp):
            def load_batch(k, par, first):
                b = 2 * k + par
                if not first:
                    sp.wait_ge(s_x_in[par], 16 * k)
                    sp.wait_ge(s_kv, b - 1)
                sp.dma_start(ctx_sb[:, par, :], ctx_in[b, :, :]).then_inc(s_ctx_in[par], 16)
                sp.dma_start(res[:, b, :], x[b, :, :]).then_inc(s_x_in[par], 16)

            def load_job(n, done):
                wait(sp, s_weight_lo, done)
                sp.dma_start(raw[:, :], packed[n, :, :]).then_inc(s_job_in, 16)
                for g in range(QG):
                    rows = slice(g * P // QG, (g + 1) * P // QG)
                    sp.dma_start(grid[rows, :, :], grids[n, g:g + 1, :, :].to_broadcast([P // QG, 2, JW])
                                 ).then_inc(s_job_in, 16)

            load_batch(0, 0, True)
            load_batch(0, 1, True)
            for k in range(3):
                sp.dma_start(grids_all[:, k, :], scales[k, :, :]).then_inc(s_grids_in, 16)
                sp.dma_start(grids_all[:, 3 + k, :], zeros[k, :, :]).then_inc(s_grids_in, 16)
            load_job(0, 0)
            with sp.Fori(1, B // 2, 1) as k:
                load_batch(k, 0, False)
                load_batch(k, 1, False)
            with sp.Fori(1, JOBS - 1, 1) as n:
                load_job(n, 2 * n)
            load_job(JOBS - 1, 2 * (JOBS - 1) - 1)
            for t in range(B):
                sp.wait_ge(s_acc, 2 * B * PAIRS + 2 * t + 2)
                sp.dma_start(out[t, :, :], res[:, t, :]).then_inc(s_out, 16)
            sp.wait_ge(s_out, 16 * B)

        @block.gpsimd
        def _(pool):
            pool.memset(neg_half[:, :], -0.5).then_inc(s_const, 1)
            pool.memset(ident[:, :], 0.0).then_inc(s_const, 1)
            pool.memset(eps[:, :], EPS).then_inc(s_const, 1)
            pool.wait_ge(s_const, 3)
            pool.affine_select(out=ident[:, :], in_=ident[:, :], compare_op=ALU.not_equal, fill=1.0,
                               base=0, pattern=[[-1, P]], channel_multiplier=1).then_inc(s_const, 1)

            def inverse_deviation(which, b, par, nth):
                pool.wait_ge(s_mv[which], b + 1)
                pool.tensor_tensor(var_eps[:, which:which + 1], mv[:, which, par, 1:2], eps[:, :],
                                   ALU.add).then_inc(s_eps, 1)
                pool.wait_ge(s_eps, nth)
                pool.tensor_tensor(rstd[:, which, par:par + 1], var_eps[:, which:which + 1],
                                   neg_half[:, :], ALU.pow).then_inc(s_rstd[which], 1)

            inverse_deviation(0, 0, 0, 1)
            inverse_deviation(0, 1, 1, 2)
            inverse_deviation(0, 2, 0, 3)
            pool.wait_ge(s_extreme, 1)
            pool.partition_all_reduce(pow2_tmp[:, 0:6], pow2[:, 0:6], P,
                                      bass.bass_isa.ReduceOp.max).then_inc(s_extreme_all, 1)
            inverse_deviation(1, 0, 0, 4)
            inverse_deviation(0, 3, 1, 5)
            inverse_deviation(1, 1, 1, 6)
            with pool.Fori(2, B // 2, 1) as k:
                for par in (0, 1):
                    b = 2 * k + par
                    inverse_deviation(0, b, par, 2 * b - 1)
                    inverse_deviation(1, b - 2, par, 2 * b)
            inverse_deviation(1, B - 2, 0, 2 * B - 1)
            inverse_deviation(1, B - 1, 1, 2 * B)

        @block.tensor
        def _(pe):
            def keys_values(k, par):
                b = 2 * k + par
                pe.wait_ge(s_ctx_in[par], 16 * k + 16)
                if isinstance(b, int) and b < 3:
                    wait(pe, s_vt_sb, b)
                else:
                    pe.wait_ge(s_xt_lo, 2 * b - 5)
                pe.matmul(ps_m[:, 0:M], qk_t[:, :], ctx_sb[:, par, :], start=True, stop=True)
                for h in range(2):
                    mm = pe.matmul(ps_m[:, M + C * h:M + C * h + C], ctx_sb[:, par, P * h:P * h + P],
                                   w_att[:, 2, :], start=True, stop=True)
                mm.then_inc(s_kv, 1)

            def probs_transposed(b, f):
                pe.wait_ge(s_prob, 2 * b + f + 1)
                wait(pe, s_prob_t_sb, 2 * b + f)
                for h in range(2):
                    for t in range(NTH):
                        mm = pe.transpose(ps_t[:, h, P * t:P * t + P],
                                          prob[:, NTH * f + t, P * h:P * h + P], ident[:, :])
                mm.then_inc(s_prob_t, 1)

            def energies(b, par, f, tiles=range(NTH)):
                if f == 0:
                    pe.wait_ge(s_xn, b + 1)
                    pe.wait_ge(s_kk_sb, b + 1)
                if tiles[0] == 0:
                    wait(pe, s_exp, 2 * b - 1 + f)
                for t in tiles:
                    n = H * f + P * t
                    mm = pe.matmul(ps_e[f][:, t, :], xn[:, par, n:n + P], kk[:, par, :],
                                   start=True, stop=True)
                if tiles[-1] == NTH - 1:
                    mm.then_inc(s_energy, 1)

            def rows_transposed(b, par, f):
                if f == 0:
                    pe.wait_ge(s_xn2, b + 1)
                    wait(pe, s_xt_lo, 2 * b)
                    if isinstance(b, int) and b == 0:
                        pe.wait_ge(s_vt_sb, 3)
                else:
                    pe.wait_ge(s_vt_sb, min(b + 4, B) if isinstance(b, int) else b + 4)
                    pe.wait_ge(s_xt_lo, 2 * b + 1)
                for j in range(J):
                    mm = pe.transpose(ps_m[:, P * j:P * j + P],
                                      xn2[:, par, 256 * j + f:256 * j + 256:2], ident[:, :])
                mm.then_inc(s_xt_ps, 1)

            def values(b, par, f):
                wait(pe, s_res, 2 * b + f)
                pe.matmul(ps_o, w_att[:, 3, :], xn[:, par, H * f:H * f + H], start=True, stop=False)
                if f == 0:
                    pe.wait_ge(s_vt_sb, b + 1)
                pe.wait_ge(s_prob_t_sb, 2 * b + f + 1)
                pe.matmul(ps_o, v_t[:, par, 0, :], prob_t[:, f, 0, :], start=False, stop=False)
                pe.matmul(ps_o, v_t[:, par, 1, :], prob_t[:, f, 1, :], start=False, stop=True
                          ).then_inc(s_att, 1)

            pe.wait_ge(s_const, 4)
            for _ in range(WARM_UP):
                pe.matmul(ps_o[:, 0:P], ident[:, :], ident[:, :], start=True, stop=True)
            pe.wait_ge(s_weights_in, 16)
            pe.matmul(ps_m[:, 0:C], w_att[:, 1, :], w_att[:, 0, :], start=True, stop=True).then_inc(s_qk, 1)
            pe.wait_ge(s_qk_sb, 1)
            keys_values(0, 0)

            def step(k, par, first=True):
                i = 2 * k + par
                a, v, r0, r1, kv = stages(i)
                if v:
                    probs_transposed(i - 1, 0)
                if r1:
                    rows_transposed(i - 3, 1 - par, 1)
                if a and first:
                    energies(i, par, 0)
                if v:
                    values(i - 1, 1 - par, 0)
                if a:
                    energies(i, par, 1, range(0, EARLY))
                if r0:
                    rows_transposed(i - 2, par, 0)
                if v:
                    probs_transposed(i - 1, 1)
                if a:
                    energies(i, par, 1, range(EARLY, NTH))
                if kv:
                    keys_values(k + par, 1 - par)
                if v:
                    values(i - 1, 1 - par, 1)

            energies(0, 0, 0)
            keys_values(0, 1)
            energies(0, 0, 1)
            energies(1, 1, 0)
            step(0, 1, first=False)
            step(1, 0)
            step(1, 1)
            with pe.Fori(2, B // 2 - 1, 1) as k:
                step(k, 0)
                step(k, 1)
            for i in range(B - 2, B + 1):
                step(i // 2, i % 2)

            def gate_up(pair, e, tb):
                u = 2 * TB * pair + TB * e + tb
                cols = slice(512 * tb, 512 * tb + 512)
                if tb == 0:
                    pe.wait_ge(s_weight_lo, 2 * (3 * pair + e) + 2)
                if isinstance(pair, int):
                    pe.wait_ge(s_xt_lo, 8 * tb + 8)
                for k, (ready, free) in enumerate(((s_gate, s_silu), (s_up, s_h))):
                    bank = ps[:, 2 * (tb % 2) + k, :]
                    wait(pe, free, u - 1)
                    n = 0
                    for odd in range(2):
                        for j in range(J):
                            for wp, xp in ((0, 0), (0, 1), (1, 0)):
                                mm = pe.matmul(bank, w_gu[:, e, wp, odd, k, j, :], xt[:, xp, odd, j, cols],
                                               start=(n == 0), stop=(n == 6 * J - 1))
                                n += 1
                    mm.then_inc(ready, 1)

            def down(pair, t, products):
                for oh in range(2):
                    g = 2 * B * pair + 2 * t + oh
                    bank = ps[:, 4 + (2 * t + oh) % 4, :]
                    wait(pe, s_acc, g - 3)
                    terms = products(slice(P * t, P * t + P), slice(NOUT * oh, NOUT * oh + NOUT))
                    for n, (h, w) in enumerate(terms):
                        mm = pe.matmul(bank, h, w, start=(n == 0), stop=(n == len(terms) - 1))
                    mm.then_inc(s_down, 1)

            def three(e, rows, o):
                return [(h_hi[:, e, rows], w_d[:, 0, e, o]), (h_hi[:, e, rows], w_d[:, 1, e, o]),
                        (h_lo[:, e, rows], w_d[:, 0, e, o])]

            def down_phase(pair, weights_done, products):
                pe.wait_ge(s_weight_lo, weights_done)
                for t in range(B):
                    if t % 4 == 0:
                        pe.wait_ge(s_h_lo, 2 * TB * pair + TB + t // 4 + 1)
                    down(pair, t, products)

            def ffn_pair(pair, first):
                for e in range(2):
                    for tb in range(TB):
                        if TB * e + tb >= first:
                            gate_up(pair, e, tb)
                down_phase(pair, 6 * pair + 6, lambda rows, o: three(0, rows, o) + three(1, rows, o))

            def gate_up_y(tb):
                u = 2 * TB * PAIRS + TB + tb
                cols = slice(512 * tb, 512 * tb + 512)
                if tb == 0:
                    pe.wait_ge(s_weight_lo, 2 * (3 * PAIRS + 1) + 2)
                pe.wait_ge(s_h, u - 1)
                n = 0
                for odd in range(2):
                    for j in range(J):
                        for wp, xp in ((0, 0), (0, 1), (1, 0)):
                            mm = pe.matmul(ps[:, 2 * (tb % 2), :], w_gu[:, 1, wp, odd, 0, j, :],
                                           xt[:, xp, odd, j, cols], start=(n == 0), stop=(n == 6 * J - 1))
                            n += 1
                mm.then_inc(s_gate, 1)

            def last_products(rows, o):
                return three(0, rows, o) + [(h_hi[:, 1, rows], w_d[:, 0, 1, o]), (h_lo[:, 1, rows], w_d[:, 0, 1, o])]

            rows_transposed(B - 2, 0, 1)
            for f in range(2):
                gate_up(0, 0, f)
                rows_transposed(B - 1, 1, f)
            ffn_pair(0, 2)
            with nc.Fori(1, PAIRS, 1, engines=[pe.engine], hint_back_edge=True) as pair:
                ffn_pair(pair, 0)
            for tb in range(TB):
                gate_up(PAIRS, 0, tb)
            for tb in range(TB):
                gate_up_y(tb)
            down_phase(PAIRS, 2 * (JOBS - 2) + 2, last_products)

        @block.scalar
        def _(act):
            act.dma_start(w_att[:, :, :], att_weights[:, :, :]).then_inc(s_weights_in, 16)
            act.wait_ge(s_qk, 1)
            act.copy(qk_t[:, :], ps_m[:, 0:C]).then_inc(s_qk_sb, 1)

            def keys_out(b, par):
                act.wait_ge(s_kv, b + 1)
                act.mul(kk[:, par, :], ps_m[:, 0:M], float(C) ** -0.5).then_inc(s_kk_sb, 1)

            def values_out(b, par):
                wait(act, s_att, 2 * b - 2)
                act.copy(v_t[:, par, :, :], ps_m[:, M:M + 2 * C].rearrange("p (h c) -> p h c", h=2)
                         ).then_inc(s_vt_sb, 1)

            def probs_out(b, f):
                act.wait_ge(s_prob_t, 2 * b + f + 1)
                act.copy(prob_t[:, f, :, :], ps_t).then_inc(s_prob_t_sb, 1)

            def exponentials(b, f):
                act.wait_ge(s_max, 2 * b + f + 1)
                for t in range(NTH):
                    ex = act.activation(prob[:, NTH * f + t, :], ps_e[f][:, t, :], ACT.Exp,
                                        bias=neg_max[:, f, t:t + 1], accum_out=total[:, f, t:t + 1])
                ex.then_inc(s_exp, 1)

            def step(k, par, meanwhile=None):
                i = 2 * k + par
                a, v, r0, r1, kv = stages(i)
                if v:
                    probs_out(i - 1, 0)
                if r1:
                    rows_hi(i - 3, 1)
                if v:
                    normalize_probs(i - 1, 1)
                if a:
                    exponentials(i, 0)
                if meanwhile:
                    meanwhile()
                if r0:
                    rows_hi(i - 2, 0)
                if v:
                    probs_out(i - 1, 1)
                if a:
                    normalize_probs(i, 0)
                if kv:
                    keys_out(i + 1, 1 - par)
                if a:
                    exponentials(i, 1)
                if kv:
                    values_out(i + 1, 1 - par)

            def rows_hi(b, f):
                act.wait_ge(s_xt_ps, 2 * b + f + 1)
                act.copy(xt[:, 0, f, :, bass.ds(b * C, C)],
                         ps_m.rearrange("p (j r) -> p j r", j=J)).then_inc(s_xt_hi, 1)

            def normalize_probs(b, f):
                act.wait_ge(s_inv, 2 * b + f + 1)
                for t in range(NTH):
                    pr = prob[:, NTH * f + t, :]
                    pn = act.activation(pr, pr, ACT.Copy, scale=inv_total[:, f, t:t + 1])
                pn.then_inc(s_prob, 1)

            def weight_hi(n, kind, nib):
                act.wait_ge(s_weight, 2 * n + nib + 1)
                src = (quant, raw)[nib][:, :].bitcast(F32)
                dst = w_d[:, 0, nib, :] if kind == 2 else w_gu[:, kind, 0, nib, :, :, :].rearrange("p k j m -> p (k j m)")
                act.copy(dst, src).then_inc(s_weight_hi, 1)

            for b in range(2):
                keys_out(b, b)
                values_out(b, b)
            exponentials(0, 0)
            normalize_probs(0, 0)
            exponentials(0, 1)
            for i in range(1, 4):
                step(i // 2, i % 2)
            with act.Fori(2, B // 2 - 1, 1) as k:
                step(k, 0)
                step(k, 1)
            step(B // 2 - 1, 0)
            weight_hi(0, 0, 0)
            step(B // 2 - 1, 1)
            step(B // 2, 0, lambda: weight_hi(0, 0, 1))
            rows_hi(B - 2, 1)

            def unit(pair, e, tb):
                u = 2 * TB * pair + TB * e + tb
                act.wait_ge(s_gate, u + 1)
                wait(act, s_h_lo, u - 1)
                act.activation(act_h[:, tb % 2, :], ps[:, 2 * (tb % 2), :], ACT.Silu,
                               scale=pow2[:, 8:9]).then_inc(s_silu, 1)
                act.wait_ge(s_h, u + 1)
                act.copy(h_hi[:, e, 512 * tb:512 * tb + 512], act_h[:, tb % 2, :]).then_inc(s_h_hi, 1)

            def ffn_pair(pair, first):
                for e in range(2):
                    for tb in range(TB):
                        if TB * e + tb >= first:
                            unit(pair, e, tb)
                        if tb >= 2 and e == 0:
                            wait(act, s_down, 2 * B * pair)
                            weight_hi(3 * pair + 2, 2, tb - 2)
                        if tb in (1, 2) and e == 1:
                            act.wait_ge(s_up, 2 * TB * pair + TB)
                            weight_hi(3 * pair + 3, 0, tb - 1)
                act.wait_ge(s_up, 2 * TB * pair + 2 * TB)
                for nib in range(2):
                    weight_hi(3 * pair + 4, 1, nib)

            for f in range(2):
                unit(0, 0, f)
                rows_hi(B - 1, f)
            for nib in range(2):
                weight_hi(1, 1, nib)
            ffn_pair(0, 2)
            with nc.Fori(1, PAIRS, 1, engines=[act.engine], hint_back_edge=True) as pair:
                ffn_pair(pair, 0)

            def last_weight_hi(y):
                act.wait_ge(s_weight, 2 * (JOBS - 2) + y + 1)
                act.copy(w_d[:, 0, y, :], quant[:, :].bitcast(F32)).then_inc(s_weight_hi, 1)

            def unit_y(tb):
                u = 2 * TB * PAIRS + TB + tb
                cols = slice(512 * tb, 512 * tb + 512)
                act.wait_ge(s_gate, u + 1)
                act.wait_ge(s_h_lo, u - 1)
                act.activation(act_h[0:HALF, tb % 2, :], ps[0:HALF, 2 * (tb % 2), :], ACT.Silu,
                               scale=pow2[0:HALF, 8:9]).then_inc(s_silu, 1)
                act.wait_ge(s_h, u + 1)
                act.copy(h_hi[HALF:P, 1, cols], act_h[0:HALF, tb % 2, :])
                act.copy(h_hi[0:HALF, 1, cols], act_h[0:HALF, tb % 2, :]).then_inc(s_h_hi, 1)

            for tb in range(TB):
                unit(PAIRS, 0, tb)
                if tb == 0:
                    act.wait_ge(s_down, 2 * B * PAIRS)
                    last_weight_hi(0)
            for tb in range(TB):
                unit_y(tb)
                if tb == 1:
                    last_weight_hi(1)

        @block.vector
        def _(dve):
            def extremes():
                dve.wait_ge(s_grids_in, 96)
                for k in range(6):
                    last = dve.tensor_reduce(pow2[:, k:k + 1], grids_all[:, k, :], X_AXIS, ALU.max,
                                             apply_absolute_value=True)
                last.then_inc(s_extreme, 1)

            def after(ins):
                count[0] += 1
                ins.then_inc(s_pow2, 1)
                dve.wait_ge(s_pow2, count[0])

            count = [0]

            def powers_of_two():
                dve.wait_ge(s_extreme_all, 1)
                after(dve.tensor_tensor(pow2_tmp[:, 0:4:3], pow2_tmp[:, 0:4:3], pow2_tmp[:, 1:5:3], ALU.max))
                after(dve.tensor_scalar(pow2_tmp[:, 3:6:2], pow2_tmp[:, 3:6:2], 15.0, None, ALU.add))
                after(dve.tensor_tensor(pow2_tmp[:, 0:3:2], pow2_tmp[:, 0:3:2], pow2_tmp[:, 3:6:2], ALU.mult))
                after(dve.tensor_scalar(pow2_tmp[:, 6:8], pow2_tmp[:, 0:3:2], 2.0 ** -60, None, ALU.max))
                bits = pow2_tmp[:, 6:8].bitcast(I32)
                after(dve.tensor_scalar(bits, bits, 0x7F800000, None, ALU.bitwise_and))
                after(dve.reciprocal(pow2[:, 6:8], pow2_tmp[:, 6:8]))
                after(dve.tensor_scalar(pow2[:, 9:10], pow2[:, 6:7], 2.0 ** -21, None, ALU.mult))
                after(dve.tensor_scalar(pow2[:, 6:8], pow2[:, 6:8], 2.0 ** 14, None, ALU.mult))
                after(dve.tensor_scalar(pow2[:, 8:9], pow2_tmp[:, 6:7], 2.0 ** -14, None, ALU.mult))
                after(dve.tensor_tensor(pow2[:, 10:11], pow2_tmp[:, 6:7], pow2_tmp[:, 6:7], ALU.mult))
                after(dve.tensor_scalar(pow2[:, 10:11], pow2[:, 10:11], pow2_tmp[:, 7:8], 2.0 ** -7,
                                        ALU.mult, ALU.mult))

            def wait_carrier():
                dve.memset(carrier[:, :], 0.0)

            def row_stats(which, b, par, src):
                wait_carrier()
                for k in range(2):
                    st = dve.bn_stats(stats[:, which, k, :], src[:, 512 * k:512 * k + 512])
                st.then_inc(s_stat[which], 1)
                dve.wait_ge(s_stat[which], b + 1)
                wait_carrier()
                dve.bn_aggr(mv[:, which, par, :], stats[:, which, :, :].rearrange("p a b -> p (a b)")
                            ).then_inc(s_mv[which], 1)

            def normalize(which, b, par, dst, src, done):
                dve.wait_ge(s_rstd[which], b + 1)
                dve.tensor_scalar(dst, src, mv[:, which, par, 0:1], rstd[:, which, par:par + 1],
                                  ALU.subtract, ALU.mult).then_inc(done, 1)

            def row(b):
                return res[:, b, :]

            def x_arrived(k, par):
                dve.wait_ge(s_x_in[par], 16 * k + 16)

            def maxima(b, f):
                dve.wait_ge(s_energy, 2 * b + f + 1)
                dve.tensor_reduce(neg_max[:, f, :], ps_e[f], X_AXIS, ALU.max, negate=True).then_inc(s_max, 1)

            def rows_lo(b, f):
                dve.wait_ge(s_xt_hi, 2 * b + f + 1)
                r = b * C
                dve.tensor_tensor(xt[:, 1, f, :, bass.ds(r, C)], ps_m.rearrange("p (j r) -> p j r", j=J),
                                  xt[:, 0, f, :, bass.ds(r, C)], ALU.subtract).then_inc(s_xt_lo, 1)

            def add_attention(b, f):
                part = res[:, b, H * f:H * f + H]
                dve.tensor_tensor(part, ps_o, part, ALU.add).then_inc(s_res, 1)

            def inverse_total(b, f):
                dve.wait_ge(s_exp, 2 * b + f + 1)
                dve.reciprocal(inv_total[:, f, :], total[:, f, :]).then_inc(s_inv, 1)

            def step(k, par, meanwhile=None):
                i = 2 * k + par
                a, v, r0, r1, kv = stages(i)
                if a:
                    maxima(i, 0)
                if r1:
                    rows_lo(i - 3, 1)
                if r0:
                    normalize(1, i - 2, par, xn2[:, par, :], row(i - 2), s_xn2)
                if kv and not (isinstance(i, int) and i == 0):
                    x_arrived(k + par, 1 - par)
                    row_stats(0, i + 1, 1 - par, row(i + 1))
                if v:
                    dve.wait_ge(s_att, 2 * (i - 1) + 1)
                    add_attention(i - 1, 0)
                if r0:
                    rows_lo(i - 2, 0)
                if a:
                    inverse_total(i, 0)
                    maxima(i, 1)
                if meanwhile:
                    meanwhile()
                if v:
                    dve.wait_ge(s_att, 2 * (i - 1) + 2)
                if kv and not (isinstance(i, int) and i == 0):
                    normalize(0, i + 1, 1 - par, xn[:, 1 - par, :], row(i + 1), s_xn)
                if v:
                    add_attention(i - 1, 1)
                    dve.wait_ge(s_res, 2 * (i - 1) + 2)
                    row_stats(1, i - 1, 1 - par, row(i - 1))
                if a:
                    inverse_total(i, 1)

            def weights(n, kind, nib, part):
                t_int = (quant, raw)[nib][:, :]
                t = t_int.bitcast(F32)
                k = 2 * n + nib + 1
                if part == 0:
                    dve.wait_ge(s_job_in, 16 * (1 + QG) * (n + 1))
                    if nib == 0:
                        dve.tensor_scalar(t_int, raw[:, :], 4, 15, ALU.logical_shift_right,
                                          ALU.bitwise_and).then_inc(s_nibble, 1)
                    else:
                        dve.tensor_scalar(t_int, raw[:, :], 15, None, ALU.bitwise_and).then_inc(s_nibble, 1)
                if part == 1:
                    dve.wait_ge(s_nibble, k)
                    dve.tensor_tensor(t, t_int, grid[:, 1, :], ALU.subtract).then_inc(s_minus_zero, 1)
                if part == 2:
                    a = 7 if kind == 2 else 6
                    dve.wait_ge(s_minus_zero, k)
                    dve.scalar_tensor_tensor(out=t, in0=t, scalar=pow2[:, a:a + 1], in1=grid[:, 0, :],
                                             op0=ALU.mult, op1=ALU.mult).then_inc(s_weight, 1)
                if part == 3:
                    dve.wait_ge(s_weight_hi, k)
                    if kind == 2:
                        hi, lo = (w_d[:, wp, nib, :] for wp in range(2))
                    else:
                        hi, lo = (w_gu[:, kind, wp, nib, :, :, :].rearrange("p k j m -> p (k j m)")
                                  for wp in range(2))
                    dve.tensor_tensor(lo, t, hi, ALU.subtract).then_inc(s_weight_lo, 1)

            for b in range(2):
                x_arrived(0, b)
                row_stats(0, b, b, row(b))
                normalize(0, b, b, xn[:, b, :], row(b), s_xn)

            def first_weights(*pieces):
                def work():
                    for nib, part in pieces:
                        weights(0, 0, nib, part)
                return work

            step(0, 0)
            extremes()
            step(0, 1, first_weights((0, 0), (0, 1)))
            step(1, 0, powers_of_two)
            step(1, 1, first_weights((0, 2)))
            with dve.Fori(2, B // 2 - 1, 1) as k:
                step(k, 0)
                step(k, 1)
            step(B // 2 - 1, 0, first_weights((1, 0), (1, 1)))
            step(B // 2 - 1, 1, first_weights((1, 2)))
            step(B // 2, 0, first_weights((0, 3), (1, 3)))
            rows_lo(B - 2, 1)

            def unit(pair, e, tb):
                u = 2 * TB * pair + TB * e + tb
                a = act_h[:, tb % 2, :]
                cols = slice(512 * tb, 512 * tb + 512)
                dve.wait_ge(s_silu, u + 1)
                dve.wait_ge(s_up, u + 1)
                dve.scalar_tensor_tensor(out=a, in0=ps[:, 2 * (tb % 2) + 1, :], scalar=pow2[:, 9:10], in1=a,
                                         op0=ALU.mult, op1=ALU.mult).then_inc(s_h, 1)
                dve.wait_ge(s_h_hi, u + 1)
                dve.tensor_tensor(h_lo[:, e, cols], a, h_hi[:, e, cols], ALU.subtract).then_inc(s_h_lo, 1)

            def add_down(pair, k):
                t, oh = k // 2, k % 2
                part = res[:, t, NOUT * oh:NOUT * oh + NOUT]
                dve.wait_ge(s_down, 2 * B * pair + k + 1)
                dve.scalar_tensor_tensor(out=part, in0=ps[:, 4 + k % 4, :], scalar=pow2[:, 10:11], in1=part,
                                         op0=ALU.mult, op1=ALU.add).then_inc(s_acc, 1)

            def ffn_pair(pair, first):
                for e in range(2):
                    for tb in range(TB):
                        if TB * e + tb >= first:
                            unit(pair, e, tb)
                        if tb >= 2 and e == 0:
                            for part in range(4):
                                weights(3 * pair + 2, 2, tb - 2, part)
                        if tb in (1, 2) and e == 1:
                            for part in range(4):
                                weights(3 * pair + 3, 0, tb - 1, part)
                for k in range(2 * B):
                    add_down(pair, k)
                    if k % 4 == 3:
                        weights(3 * pair + 4, 1, k // 16, k // 4 % 4)

            normalize(1, B - 1, 1, xn2[:, 1, :], row(B - 1), s_xn2)
            for f in range(2):
                unit(0, 0, f)
                rows_lo(B - 1, f)
            for nib in range(2):
                for part in range(4):
                    weights(1, 1, nib, part)
            ffn_pair(0, 2)
            with nc.Fori(1, PAIRS, 1, engines=[dve.engine], hint_back_edge=True) as pair:
                ffn_pair(pair, 0)

            def last_weights(y, part):
                k = 2 * (JOBS - 2) + y + 1
                t_int = quant[:, :]
                t = t_int.bitcast(F32)
                if part == 0:
                    dve.wait_ge(s_job_in, 16 * (1 + QG) * (JOBS - 1 + y))
                    size = P // 4 if y else P // 2
                    for lo in range(0, P, 2 * size):
                        dve.tensor_scalar(t_int[lo:lo + size, :], raw[lo:lo + size, :], 4, 15,
                                          ALU.logical_shift_right, ALU.bitwise_and)
                        nibble = dve.tensor_scalar(t_int[lo + size:lo + 2 * size, :],
                                                   raw[lo + size:lo + 2 * size, :], 15, None, ALU.bitwise_and)
                    nibble.then_inc(s_nibble, 1)
                if part == 1:
                    dve.wait_ge(s_nibble, k)
                    dve.tensor_tensor(t, t_int, grid[:, 1, :], ALU.subtract).then_inc(s_minus_zero, 1)
                if part == 2:
                    dve.wait_ge(s_minus_zero, k)
                    dve.scalar_tensor_tensor(out=t, in0=t, scalar=pow2[:, 7:8], in1=grid[:, 0, :],
                                             op0=ALU.mult, op1=ALU.mult).then_inc(s_weight, 1)
                if part == 3:
                    dve.wait_ge(s_weight_hi, k)
                    rows = slice(HALF, P) if y else slice(0, P)
                    lo = w_d[rows, 0, 1, :] if y else w_d[rows, 1, 0, :]
                    dve.tensor_tensor(lo, t[rows, :], w_d[rows, 0, y, :], ALU.subtract).then_inc(s_weight_lo, 1)

            def unit_y(tb):
                u = 2 * TB * PAIRS + TB + tb
                a = act_h[0:HALF, tb % 2, :]
                cols = slice(512 * tb, 512 * tb + 512)
                dve.wait_ge(s_silu, u + 1)
                dve.scalar_tensor_tensor(out=a, in0=ps[HALF:P, 2 * (tb % 2), :], scalar=pow2[HALF:P, 9:10], in1=a,
                                         op0=ALU.mult, op1=ALU.mult).then_inc(s_h, 1)
                dve.wait_ge(s_h_hi, u + 1)
                dve.tensor_tensor(h_lo[0:HALF, 1, cols], a, h_hi[0:HALF, 1, cols], ALU.subtract).then_inc(s_h_lo, 1)

            for tb in range(TB):
                unit(PAIRS, 0, tb)
                if tb == 0:
                    for part in range(4):
                        last_weights(0, part)
            dve.memset(shared[HALF:P, 2048 + 1024:2048 + 2048], 0.0)
            for tb in range(TB):
                unit_y(tb)
                if tb == 0:
                    last_weights(1, 0)
                    last_weights(1, 1)
                if tb == 1:
                    last_weights(1, 2)
                    last_weights(1, 3)
            for k in range(2 * B):
                add_down(PAIRS, k)


def kernel(x, ctx_1024, L0_xattn_Wq, L0_xattn_Wk, L0_xattn_Wv, L0_xattn_Wskip, L0_ffn_gate_Wq, L0_ffn_up_Wq,
           L0_ffn_down_Wq, L0_ffn_gate_scale, L0_ffn_gate_zero, L0_ffn_up_scale, L0_ffn_up_zero,
           L0_ffn_down_scale, L0_ffn_down_zero):
    import concourse.bacc as bacc
    from concourse.bass_utils import run_bass_kernel_spmd

    cut = PAIRS * 256
    cut_y = cut + P

    def gate_up_layout(gate, up, rows):
        a = np.stack([np.asarray(gate), np.asarray(up)])
        a = a.reshape(2, INTER, J, rows)
        full = a[:, :cut].reshape(2, PAIRS, P, 2, J, rows).transpose(1, 3, 5, 0, 4, 2)
        tile_x = a[:, cut:cut_y].reshape(2, P // 2, 2, J, rows).transpose(4, 0, 3, 2, 1)
        tile_y = a[:, cut_y:].reshape(2, P // 4, 2, J, rows).transpose(4, 3, 0, 2, 1).reshape(rows, 1, J, P)
        tile_y = np.concatenate([tile_y, np.zeros_like(tile_y)], axis=1)
        return full.reshape(PAIRS, 2, rows, JW), tile_x.reshape(1, rows, JW), tile_y.reshape(1, rows, JW)

    def down_layout(a, rows):
        a = np.asarray(a).T
        x0, y0 = PAIRS * rows, PAIRS * rows + rows // 2
        return a[:x0].reshape(PAIRS, 1, rows, N), np.tile(a[x0:y0], (2, 1))[None], np.tile(a[y0:], (4, 1))[None]

    def jobs(gate, up, down, rows):
        pairs_gu, x_gu, y_gu = gate_up_layout(gate, up, rows)
        pairs_d, x_d, y_d = down_layout(down, rows)
        pairs = np.concatenate([pairs_gu, pairs_d], axis=1).reshape(3 * PAIRS, rows, JW)
        return np.concatenate([pairs, x_gu, y_gu, x_d, y_d])

    packed = jobs(L0_ffn_gate_Wq, L0_ffn_up_Wq, L0_ffn_down_Wq, P)
    grids = np.stack([jobs(L0_ffn_gate_scale, L0_ffn_up_scale, L0_ffn_down_scale, QG),
                      jobs(L0_ffn_gate_zero, L0_ffn_up_zero, L0_ffn_down_zero, QG)], axis=2)
    arrays = {
        "x": np.asarray(x),
        "ctx": np.asarray(ctx_1024),
        "att_weights": np.stack([np.asarray(L0_xattn_Wq), np.asarray(L0_xattn_Wk), np.asarray(L0_xattn_Wv).T,
                                 np.asarray(L0_xattn_Wskip).T], axis=1),
        "packed": packed,
        "grids": grids,
        "scales": np.stack([np.asarray(a).reshape(P, -1) for a in
                            (L0_ffn_gate_scale, L0_ffn_up_scale, L0_ffn_down_scale)]),
        "zeros": np.stack([np.asarray(a).reshape(P, -1) for a in
                           (L0_ffn_gate_zero, L0_ffn_up_zero, L0_ffn_down_zero)]),
    }
    arrays = {k: np.ascontiguousarray(a) for k, a in arrays.items()}
    nc = bacc.Bacc("TRN2", target_bir_lowering=False, num_devices=1)
    args = [nc.dram_tensor(k, a.shape, mybir.dt.from_np(a.dtype), kind="ExternalInput").ap()
            for k, a in arrays.items()]
    out = nc.dram_tensor("out", (B, C, N), F32, kind="ExternalOutput").ap()
    build(nc, *args, out)
    r = run_bass_kernel_spmd(nc, [arrays], core_ids=[0])
    return r.results[0]["out"]
```
